# Optimizing a Trainium2 kernel written in Bass

```python
import numpy as np
import jax
import jax.numpy as jnp

def _softmax(x, axis=-1):
    return jax.nn.softmax(x, axis=axis)

def _gelu(x):
    return jax.nn.gelu(x, approximate=True)

def _silu(x):
    return jax.nn.silu(x)

def _sigmoid(x):
    return jax.nn.sigmoid(x)

def _layernorm(x, axis=-1, eps=1e-05):
    m = jnp.mean(x, axis=axis, keepdims=True)
    v = jnp.var(x, axis=axis, keepdims=True)
    return (x - m) / jnp.sqrt(v + eps)

def _scatter_add(tgt, idx, src, axis=0):
    return tgt.at[idx].add(src)

def _segment_sum(src, seg, n):
    return jax.ops.segment_sum(src, seg, n)
kernel_name = 'mk_adj_preln_d1_adj_r2_bc9330'

def setup_inputs(seed: int=0):
    np.random.seed(seed)
    _w = jnp.asarray

    def _rec_inputs():
        import jax
        import jax.numpy as jnp
        _gk = jax.random.key(seed)
        x = -0.0002928 + 1 * jax.random.normal(jax.random.fold_in(_gk, 1), (64, 128, 256), jnp.float32)
        _a = jax.random.bernoulli(jax.random.fold_in(_gk, 2), 0.125, (64, 128, 128))
        adj = _a.astype(jnp.int32)
        return (x, adj)
    x, adj = _rec_inputs()

    def _L0_gnn_setup():
        import jax, jax.numpy as jnp
        import numpy as np
        L = 3
        D = 256
        B, N = (8, 512)
        EPS = 1e-05

        def layernorm(x, gamma, beta):
            mu = jnp.mean(x, axis=-1, keepdims=True)
            var = jnp.var(x, axis=-1, keepdims=True)
            return (x - mu) * jax.lax.rsqrt(var + EPS) * gamma + beta
        key = jax.random.key(seed)
        ks = jax.random.split(key, 12)
        s = 1.0 / np.sqrt(D)
        node_features = jax.random.normal(ks[0], (B, N, D), dtype=jnp.float32)
        adjacency_matrix = jax.random.randint(ks[1], (B, N, N), 0, 2, dtype=jnp.int32)
        return {'node_features': node_features, 'adjacency_matrix': adjacency_matrix, 'attn_w': jax.random.normal(ks[2], (L, 2 * D), dtype=jnp.float32) * (1.0 / np.sqrt(2 * D)), 'attn_b': jax.random.normal(ks[3], (L,), dtype=jnp.float32) * 0.01, 'W1': jax.random.normal(ks[4], (L, D, 4 * D), dtype=jnp.float32) * s, 'b1': jnp.zeros((L, 4 * D), dtype=jnp.float32), 'W2': jax.random.normal(ks[5], (L, 4 * D, D), dtype=jnp.float32) * (1.0 / np.sqrt(4 * D)), 'b2': jnp.zeros((L, D), dtype=jnp.float32), 'g1': jnp.ones((L, D), dtype=jnp.float32), 'beta1': jnp.zeros((L, D), dtype=jnp.float32), 'g2': jnp.ones((L, D), dtype=jnp.float32), 'beta2': jnp.zeros((L, D), dtype=jnp.float32)}
    _L0_gnn_all = _L0_gnn_setup()
    _L0_gnn_in = {k: v for k, v in _L0_gnn_all.items() if k in ('attn_w', 'attn_b', 'W1', 'b1', 'W2', 'b2', 'g1', 'beta1', 'g2', 'beta2')}
    del _L0_gnn_all
    return {'x': x, 'adj': adj, 'L0_gnn_attn_w': _L0_gnn_in['attn_w'], 'L0_gnn_attn_b': _L0_gnn_in['attn_b'], 'L0_gnn_W1': _L0_gnn_in['W1'], 'L0_gnn_b1': _L0_gnn_in['b1'], 'L0_gnn_W2': _L0_gnn_in['W2'], 'L0_gnn_b2': _L0_gnn_in['b2'], 'L0_gnn_g1': _L0_gnn_in['g1'], 'L0_gnn_beta1': _L0_gnn_in['beta1'], 'L0_gnn_g2': _L0_gnn_in['g2'], 'L0_gnn_beta2': _L0_gnn_in['beta2']}

def reference(x, adj, L0_gnn_attn_w, L0_gnn_attn_b, L0_gnn_W1, L0_gnn_b1, L0_gnn_W2, L0_gnn_b2, L0_gnn_g1, L0_gnn_beta1, L0_gnn_g2, L0_gnn_beta2):
    import jax
    import jax.numpy as jnp

    def _L0_gnn_ref(node_features, adjacency_matrix, attn_w, attn_b, W1, b1, W2, b2, g1, beta1, g2, beta2):
        import jax, jax.numpy as jnp
        import numpy as np
        L = 3
        D = 256
        B, N = (8, 512)
        EPS = 1e-05

        def layernorm(x, gamma, beta):
            mu = jnp.mean(x, axis=-1, keepdims=True)
            var = jnp.var(x, axis=-1, keepdims=True)
            return (x - mu) * jax.lax.rsqrt(var + EPS) * gamma + beta
        n = adjacency_matrix.shape[-1]
        mask = adjacency_matrix.astype(jnp.float32) + jnp.eye(n, dtype=jnp.float32) > 0
        x = node_features
        d = x.shape[-1]
        for l in range(attn_w.shape[0]):
            si = x @ attn_w[l, :d]
            sj = x @ attn_w[l, d:]
            scores = si[:, :, None] + sj[:, None, :] + attn_b[l]
            scores = jnp.where(scores >= 0, scores, 0.2 * scores)
            scores = jnp.where(mask, scores, -jnp.inf)
            attn = jax.nn.softmax(scores, axis=-1)
            agg = jnp.einsum('bij,bjd->bid', attn, x)
            h = layernorm(x + agg, g1[l], beta1[l])
            ff = jax.nn.gelu(h @ W1[l] + b1[l], approximate=False) @ W2[l] + b2[l]
            x = layernorm(h + ff, g2[l], beta2[l])
        return x
    h = jnp.maximum(_layernorm(x, axis=-1), 0.0)
    x = x + _L0_gnn_ref(h, adj, L0_gnn_attn_w, L0_gnn_attn_b, L0_gnn_W1, L0_gnn_b1, L0_gnn_W2, L0_gnn_b2, L0_gnn_g1, L0_gnn_beta1, L0_gnn_g2, L0_gnn_beta2)
    return x

_drawn_inputs = setup_inputs


def setup_inputs(seed=0):
    import zlib

    import numpy as np

    out = dict(_drawn_inputs(seed))
    spreads = {'L0_gnn_b1': (0.0, 0.1),
     'L0_gnn_b2': (0.0, 0.1),
     'L0_gnn_g1': (1.0, 0.2),
     'L0_gnn_beta1': (0.0, 0.1),
     'L0_gnn_g2': (1.0, 0.2),
     'L0_gnn_beta2': (0.0, 0.1)}
    factors = {'L0_gnn_attn_b': 64.0}
    for name, (base, spread) in spreads.items():
        noise = np.random.default_rng([zlib.crc32(name.encode()), seed]).standard_normal(out[name].shape)
        drawn = base * np.exp(spread * noise) if base else spread * noise
        out[name] = jnp.asarray(drawn.astype(out[name].dtype))
    for name, factor in factors.items():
        out[name] = (out[name] * factor).astype(out[name].dtype)
    return out
```

```python
from contextlib import ExitStack

import concourse.bass as bass
from concourse import mybir
from concourse.alu_op_type import AluOpType as ALU

ACT = mybir.ActivationFunctionType
AX_X = mybir.AxisListType.X
F32 = mybir.dt.float32
F32R = mybir.dt.float32r
BF16 = mybir.dt.bfloat16
I32 = mybir.dt.int32

P = 128
GPI = 4
TOK = GPI * P
EPS = 1e-5
SLOPE = 0.2
BIG = 3.0e38
LAG = 2


def gnn_kernel(nc, x, adj, attn_w, attn_b, W1, b1, W2, b2, g1, beta1, g2, beta2, out):
    B, N, D = x.shape
    L, _, HID = W1.shape
    assert N == P and D % P == 0 and HID % P == 0 and B % GPI == 0
    ITEMS = B // GPI
    KD = D // P
    KH = HID // P
    BANKS = GPI * D // 512
    PER = GPI // BANKS
    STEPS = L * ITEMS
    assert KH % 4 == 0 and ITEMS % 2 == 0 and BANKS == 2 and KD == 2 and GPI * P == 512

    with ExitStack() as ctx:
        def sb(name, shape, dt=F32):
            return ctx.enter_context(nc.sbuf_tensor(name, shape, dt))

        def ps(name, shape):
            return ctx.enter_context(nc.psum_tensor(name, shape, F32))

        def sem(name):
            return ctx.enter_context(nc.semaphore(name))

        xs = sb("xs", [P, ITEMS, GPI, D])
        masked = sb("masked", [P, ITEMS, GPI, P], BF16)
        sij = sb("sij", [P, ITEMS, 2 * GPI])
        W1hi = sb("W1hi", [P, KD, HID], F32R)
        W1lo = sb("W1lo", [P, KD, HID], F32R)
        W2hi = sb("W2hi", [P, KH, D], F32R)
        W2lo = sb("W2lo", [P, KH, D], F32R)
        W1raw = sb("W1raw", [P, KD, HID])
        W2raw = sb("W2raw", [P, KH, D])
        aw = sb("aw", [P, L, 2, D])
        ab = sb("ab", [P, L])
        g2r = sb("g2r", [P, L, D])
        be2r = sb("be2r", [P, L, D])
        b1c = sb("b1c", [P, L, KH])
        g1c = sb("g1c", [P, L, KD])
        be1c = sb("be1c", [P, L, KD])
        b2c = sb("b2c", [P, L, KD])
        beb2 = sb("beb2", [P, L, KD])
        ident = sb("ident", [P, P])
        xin = sb("xin", [P, GPI, D])
        adjin = sb("adjin", [P, GPI, P], I32)
        ssc = sb("ssc", [P, 2, 2 * GPI])
        t = sb("t", [P, GPI, P])
        e = sb("e", [P, GPI, P])
        eT = sb("eT", [P, GPI, P])
        tmax = sb("tmax", [P, GPI])
        negm = sb("negm", [P, GPI])
        den = sb("den", [P, GPI])
        rden = sb("rden", [P, GPI])
        r = sb("r", [P, GPI, D])
        hT = sb("hT", [P, KD, TOK])
        hTb = sb("hTb", [P, KD, TOK])
        Hhi = [sb(f"Hhi{b}", [P, KD, TOK], F32R) for b in range(2)]
        Hlo = [sb(f"Hlo{b}", [P, KD, TOK], F32R) for b in range(2)]
        G = sb("G", [P, 2, TOK])
        Ghi = [sb(f"Ghi{b}", [P, TOK], F32R) for b in range(4)]
        Glo = [sb(f"Glo{b}", [P, TOK], F32R) for b in range(4)]
        junk = sb("junk", [P, 2, D], BF16)
        st0 = sb("st0", [P, GPI, 6])
        st1 = sb("st1", [P, GPI, 6])
        st2 = sb("st2", [P, GPI, 6])
        mv0 = sb("mv0", [P, GPI, 2])
        mv1 = sb("mv1", [P, GPI, 2])
        mv2 = sb("mv2", [P, GPI, 2])
        ve0 = sb("ve0", [P, GPI])
        ve1 = sb("ve1", [P, GPI])
        ve2 = sb("ve2", [P, GPI])
        rs0 = sb("rs0", [P, GPI])
        rs1 = sb("rs1", [P, GPI])
        rs2 = sb("rs2", [P, GPI])
        nmr = sb("nmr", [P, GPI])
        mhalf = sb("mhalf", [P, GPI])
        epsc = sb("epsc", [P, GPI])

        U = ps("U", [P, 2, 512])
        F = ps("F", [P, 2, BANKS, 512])
        T = ps("T", [P, 2, 512])

        s_const = sem("s_const")
        s_const2 = sem("s_const2")
        s_w1raw = sem("s_w1raw")
        s_w2raw = sem("s_w2raw")
        s_xin = sem("s_xin")
        s_adj = sem("s_adj")
        s_out = sem("s_out")
        s_id = sem("s_id")
        w1_ready = sem("w1_ready")
        w2_ready = sem("w2_ready")
        beb2_ready = sem("beb2_ready")
        w_hi = sem("w_hi")
        in_bn = sem("in_bn")
        in_mv = sem("in_mv")
        in_rs = sem("in_rs")
        in_nmr = sem("in_nmr")
        x0_done = sem("x0_done")
        mask_done = sem("mask_done")
        mask_ready = sem("mask_ready")
        dots0_done = sem("dots0_done")
        dots_done = sem("dots_done")
        s0_ready = sem("s0_ready")
        s_ready = sem("s_ready")
        s_copied = sem("s_copied")
        sjb_ready = sem("sjb_ready")
        t_ready = sem("t_ready")
        max_steps = sem("max_steps")
        exp_done = sem("exp_done")
        et_ready = sem("et_ready")
        et_copied = sem("et_copied")
        rden_ready = sem("rden_ready")
        agg_ready = sem("agg_ready")
        r_done = sem("r_done")
        bn1 = sem("bn1")
        mv1_done = sem("mv1_done")
        rs1_steps = sem("rs1_steps")
        n1_done = sem("n1_done")
        ht_psum = sem("ht_psum")
        h_act = sem("h_act")
        h_lo = sem("h_lo")
        h_b2 = sem("h_b2")
        f_open = sem("f_open")
        u_ready = sem("u_ready")
        gelu_done = sem("gelu_done")
        glo_ready = sem("glo_ready")
        w2_done = sem("w2_done")
        bn2 = sem("bn2")
        mv2_done = sem("mv2_done")
        f_free = sem("f_free")
        rs2_steps = sem("rs2_steps")
        x_done = sem("x_done")
        o_ready = sem("o_ready")

        x_g = x.rearrange("(i q) n d -> i n q d", q=GPI)
        out_g = out.rearrange("(i q) n d -> i n q d", q=GPI)
        adj_g = adj.rearrange("(i q) n m -> i n q m", q=GPI)
        CONSTS, CONSTS2 = 2, 6

        def steps(engine, body):
            for l in range(L):
                head = 3 if l == 0 else 1
                tail = ITEMS - 3 if l in (0, L - 1) else ITEMS - 1
                for i in range(head):
                    body(l, i, i % 2)
                with engine.Fori(0, (tail - head) // 2) as j:
                    body(l, 2 * j + head, 1)
                    body(l, 2 * j + head + 1, 0)
                for i in range(tail, ITEMS):
                    body(l, i, i % 2)

        def at(l, i, off):
            n = l * ITEMS + i + off
            if isinstance(n, int) and not 0 <= n < STEPS:
                return None
            return n

        def group(l, i, off):
            if isinstance(i, int):
                return (i + off) % ITEMS
            return i + off if off < 2 else (i + off) % ITEMS

        def layer(l, i, off):
            return (l * ITEMS + i + off) // ITEMS if isinstance(i, int) else l

        def has_features(l, i):
            return l == 0 and (not isinstance(i, int) or i + 3 < ITEMS)

        def after(engine, semaphore, value):
            if not isinstance(value, int) or value > 0:
                engine.wait_ge(semaphore, value)

        block = ctx.enter_context(nc.Block())

        @block.sync
        def _(sp):
            def load(n):
                if not (isinstance(n, int) and n == 0):
                    sp.wait_ge(x0_done, GPI * n)
                    sp.wait_ge(mask_done, n)
                sp.dma_start(xin[:, :, :], x_g[n, :, :, :]).then_inc(s_xin, 16)
                sp.dma_start(adjin[:, :, :], adj_g[n, :, :, :]).then_inc(s_adj, 16)

            load(0)
            sp.dma_start(aw[:, :, :, :].rearrange("p l a d -> p (l a d)"),
                         attn_w.rearrange("l a -> (l a)").partition_broadcast(P)).then_inc(s_const, 16)
            sp.dma_start(ab[:, :], attn_b.partition_broadcast(P)).then_inc(s_const, 16)
            sp.dma_start(W1raw[:, :, :], W1[0].rearrange("(k p) f -> p k f", p=P)).then_inc(s_w1raw, 16)
            sp.dma_start(W2raw[:, :, :], W2[0].rearrange("(c p) d -> p c d", p=P)).then_inc(s_w2raw, 16)
            load(1)
            for dst, src in ((g1c, g1), (be1c, beta1), (b2c, b2), (b1c, b1)):
                sp.dma_start(dst[:, :, :], src.rearrange("l (k p) -> p l k", p=P),
                             allow_slow_non_contiguous=True).then_inc(s_const2, 16)
            for dst, src in ((g2r, g2), (be2r, beta2)):
                sp.dma_start(dst[:, :, :].rearrange("p l d -> p (l d)"),
                             src.rearrange("l d -> (l d)").partition_broadcast(P)).then_inc(s_const2, 16)
            with sp.Fori(2, ITEMS) as n:
                load(n)

            def load_weights(l):
                sp.wait_ge(w1_ready, KH * l)
                sp.wait_ge(w2_ready, KH * l)
                sp.dma_start(W1raw[:, :, :], W1[l].rearrange("(k p) f -> p k f", p=P)).then_inc(s_w1raw, 16)
                sp.dma_start(W2raw[:, :, :], W2[l].rearrange("(c p) d -> p c d", p=P)).then_inc(s_w2raw, 16)

            for l in range(1, L):
                load_weights(l)
            sp.wait_ge(x0_done, GPI * ITEMS)
            sp.dma_start(xin[:, :, :], x_g[0, :, :, :]).then_inc(s_xin, 16)
            with sp.Fori(0, ITEMS - 1) as g:
                sp.wait_ge(o_ready, g + 1)
                sp.dma_start(xin[:, :, :], x_g[g + 1, :, :, :]).then_inc(s_xin, 16)
                sp.dma_start(out_g[g, :, :, :], xs[:, g, :, :]).then_inc(s_out, 16)
            sp.wait_ge(o_ready, ITEMS)
            sp.dma_start(out_g[ITEMS - 1, :, :, :], xs[:, ITEMS - 1, :, :]).then_inc(s_out, 16)
            sp.wait_ge(s_out, 16 * ITEMS)

        @block.gpsimd
        def _(pool):
            nc.gpsimd.memset(ident[:, :], 0.0).then_inc(s_id, 1)
            nc.gpsimd.memset(mhalf[:, :], -0.5).then_inc(s_id, 1)
            nc.gpsimd.memset(epsc[:, :], EPS).then_inc(s_id, 1)
            pool.wait_ge(s_id, 3)
            nc.gpsimd.affine_select(out=ident[:, :], in_=ident[:, :], compare_op=ALU.not_equal, fill=1.0,
                                    base=0, pattern=[[-1, P]], channel_multiplier=1).then_inc(s_id, 1)

            def rstd(n, mv, mv_done, ve, rs, steps_sem):
                pool.wait_ge(mv_done, GPI * (n + 1))
                nc.gpsimd.tensor_tensor(ve[:, :], mv[:, :, 1], epsc[:, :], ALU.add).then_inc(steps_sem, 1)
                pool.wait_ge(steps_sem, 2 * n + 1)
                nc.gpsimd.tensor_tensor(rs[:, :], ve[:, :], mhalf[:, :], ALU.pow).then_inc(steps_sem, 1)

            def split_w1(l, c):
                cols = slice(c * P, (c + 1) * P)
                if l:
                    pool.wait_ge(u_ready, KH * (ITEMS * l - 1) + c + 1)
                nc.gpsimd.tensor_copy(W1hi[:, :, cols], W1raw[:, :, cols]).then_inc(w_hi, 1)
                pool.wait_ge(w_hi, 2 * (KH * l + c) + 1)
                nc.gpsimd.tensor_tensor(W1lo[:, :, cols], W1raw[:, :, cols], W1hi[:, :, cols].bitcast(F32),
                                        ALU.subtract).then_inc(w1_ready, 1)

            def split_w2(l, c):
                if l:
                    pool.wait_ge(w2_done, KH * (ITEMS * l - 1) + c + 1)
                nc.gpsimd.tensor_copy(W2hi[:, c, :], W2raw[:, c, :]).then_inc(w_hi, 1)
                pool.wait_ge(w_hi, 2 * (KH * l + c) + 2)
                nc.gpsimd.tensor_tensor(W2lo[:, c, :], W2raw[:, c, :], W2hi[:, c, :].bitcast(F32),
                                        ALU.subtract).then_inc(w2_ready, 1)

            def split_layer(l, chunks=range(KH)):
                pool.wait_ge(s_w1raw, 16 * (l + 1))
                pool.wait_ge(s_w2raw, 16 * (l + 1))
                for c in chunks:
                    split_w1(l, c)
                    split_w2(l, c)

            def split_h(n, p):
                after(pool, u_ready, KH * (n - 1))
                for k in range(KD):
                    pool.wait_ge(h_act, 2 * (KD * n + k) + 2)
                    nc.gpsimd.tensor_tensor(Hlo[p][:, k, :], hT[:, k, :], Hhi[p][:, k, :].bitcast(F32),
                                            ALU.subtract).then_inc(h_lo, 1)

            rstd(0, mv0, in_mv, ve0, rs0, in_rs)
            split_layer(0, range(0, 3))
            rstd(1, mv0, in_mv, ve0, rs0, in_rs)
            split_layer(0, range(3, 5))
            rstd(0, mv1, mv1_done, ve1, rs1, rs1_steps)
            rstd(2, mv0, in_mv, ve0, rs0, in_rs)
            split_h(0, 0)
            split_layer(0, range(5, KH))

            def output(n, g):
                pool.wait_ge(x_done, GPI * (n + 1))
                pool.wait_ge(s_xin, 16 * (ITEMS + g + 1))
                nc.gpsimd.tensor_tensor(xs[:, g, :, :], xs[:, g, :, :], xin[:, :, :], ALU.add).then_inc(o_ready, 1)

            def body(l, i, p):
                if at(l, i, 1) is not None:
                    rstd(at(l, i, 1), mv1, mv1_done, ve1, rs1, rs1_steps)
                if l > 0 and isinstance(i, int) and i == 0:
                    split_layer(l, range(KH - 4, KH - 2))
                if has_features(l, i):
                    rstd(i + 3, mv0, in_mv, ve0, rs0, in_rs)
                if at(l, i, -1) is not None:
                    rstd(at(l, i, -1), mv2, mv2_done, ve2, rs2, rs2_steps)
                if at(l, i, 1) is not None:
                    split_h(at(l, i, 1), 1 - p)
                if at(l, i, -1) is not None:
                    if layer(l, i, -1) == L - 1:
                        output(at(l, i, -1), group(l, i, -1))
                    if isinstance(i, int) and i == 0:
                        split_layer(l, range(KH - 2, KH))
                if isinstance(i, int) and i == ITEMS - 1 and l < L - 1:
                    split_layer(l + 1, range(0, KH - 4))

            steps(pool, body)
            rstd(STEPS - 1, mv2, mv2_done, ve2, rs2, rs2_steps)
            output(STEPS - 1, ITEMS - 1)

        @block.scalar
        def _(act):
            def features(n):
                act.wait_ge(in_nmr, n + 1)
                for q in range(GPI):
                    nc.scalar.activation(xs[:, n, q, :], xin[:, q, :], ACT.Relu, bias=nmr[:, q:q + 1],
                                         scale=rs0[:, q:q + 1]).then_inc(x0_done, 1)

            def exps(n):
                act.wait_ge(max_steps, 3 * (n + 1))
                after(act, et_ready, n)
                after(act, rden_ready, n)
                for q in range(GPI):
                    nc.scalar.activation(e[:, q, :], t[:, q, :], ACT.Exp, bias=negm[:, q:q + 1],
                                         accum_out=den[:, q:q + 1]).then_inc(exp_done, 1)

            def copy_eT(n):
                act.wait_ge(et_ready, n + 1)
                after(act, agg_ready, BANKS * n)
                nc.scalar.copy(eT[:, :, :], T[:, 1, :].rearrange("p (q j) -> p q j", q=GPI)).then_inc(et_copied, 1)

            def affine_h(n, l, p):
                after(act, h_lo, KD * n)
                after(act, u_ready, KH * (n - 1))
                for k in range(KD):
                    act.wait_ge(ht_psum, KD * n + k + 1)
                    for dst in (hT, Hhi[p]):
                        nc.scalar.activation(dst[:, k, :], T[:, k, :], ACT.Identity, bias=be1c[:, l, k:k + 1],
                                             scale=g1c[:, l, k:k + 1]).then_inc(h_act, 1)

            def affine_hb(n, l):
                after(act, f_open, n)
                for k in range(KD):
                    nc.scalar.activation(hTb[:, k, :], T[:, k, :], ACT.Identity, bias=beb2[:, l, k:k + 1],
                                         scale=g1c[:, l, k:k + 1]).then_inc(h_b2, 1)

            def gelu(n, l, c):
                m = KH * n + c
                act.wait_ge(u_ready, m + 1)
                after(act, glo_ready, m - 1)
                nc.scalar.activation(G[:, c % 2, :], U[:, c % 2, :], ACT.Gelu, bias=b1c[:, l, c:c + 1]).then_inc(gelu_done, 1)
                after(act, w2_done, m - 3)
                nc.scalar.activation(Ghi[c % 4][:, :], U[:, c % 2, :], ACT.Gelu, bias=b1c[:, l, c:c + 1]).then_inc(gelu_done, 1)

            features(0)
            exps(0)
            copy_eT(0)
            features(1)
            act.wait_ge(s_const2, 16 * CONSTS2)
            affine_h(0, 0, 0)
            act.wait_ge(beb2_ready, 1)
            affine_hb(0, 0)
            features(2)
            exps(1)

            def body(l, i, p):
                for c in range(KH):
                    gelu(at(l, i, 0), l, c)
                    if c == 0 and at(l, i, 1) is not None:
                        copy_eT(at(l, i, 1))
                    if c == 4 and at(l, i, 1) is not None:
                        affine_h(at(l, i, 1), layer(l, i, 1), 1 - p)
                    if c == 5 and at(l, i, 1) is not None:
                        affine_hb(at(l, i, 1), layer(l, i, 1))
                    if c == 6 and has_features(l, i):
                        features(i + 3)
                    if c == 7 and at(l, i, 2) is not None:
                        exps(at(l, i, 2))

            steps(act, body)

        @block.vector
        def _(dve):
            dve.wait_ge(s_id, 4)

            def dots(m, g, l, a, done, ready):
                for q in range(GPI):
                    if a * GPI + q >= 2:
                        dve.wait_ge(done, 2 * GPI * m + a * GPI + q - 1)
                    nc.vector.scalar_tensor_tensor(
                        out=junk[:, q % 2, :], in0=xs[:, g, q, :], scalar=1.0, in1=aw[:, l, a, :], op0=ALU.mult,
                        op1=ALU.mult, accum_out=sij[:, g, a * GPI + q:a * GPI + q + 1]).then_inc(done, 1)
                if a == 1:
                    dve.wait_ge(done, 2 * GPI * (m + 1))
                    nc.vector.tensor_scalar(sij[:, g, 0:GPI], sij[:, g, 0:GPI], ab[:, l:l + 1], None,
                                            ALU.add).then_inc(ready, 1)

            def statistics0(n):
                dve.wait_ge(s_xin, 16 * (n + 1))
                for q in range(GPI):
                    nc.vector.bn_stats(st0[:, q, :], xin[:, q, :]).then_inc(in_bn, 1)

            def aggregate0(n):
                for q in range(GPI):
                    nc.vector.bn_aggr(mv0[:, q, :], st0[:, q, :]).then_inc(in_mv, 1)

            def minus_mean(n):
                dve.wait_ge(in_rs, 2 * n + 2)
                nc.vector.scalar_tensor_tensor(out=nmr[:, :], in0=mv0[:, :, 0], scalar=-1.0, in1=rs0[:, :],
                                               op0=ALU.mult, op1=ALU.mult).then_inc(in_nmr, 1)

            def mask(n):
                dve.wait_ge(s_adj, 16 * (n + 1))
                nc.vector.scalar_tensor_tensor(
                    out=masked[:, n, :, :], in0=adjin[:, :, :], scalar=-1.0,
                    in1=ident[:, :].unsqueeze(1).broadcast_to([P, GPI, P]), op0=ALU.mult,
                    op1=ALU.is_ge).then_inc(mask_done, 1)

            def scale_mask(n):
                dve.wait_ge(mask_done, n + 1)
                nc.vector.tensor_scalar(masked[:, n, :, :], masked[:, n, :, :], -BIG, None, ALU.mult).then_inc(mask_ready, 1)

            def features(n):
                statistics0(n)
                dve.wait_ge(in_bn, GPI * (n + 1))
                aggregate0(n)
                mask(n)
                minus_mean(n)
                scale_mask(n)

            def first_dots(n, a):
                if a == 0:
                    dve.wait_ge(x0_done, GPI * (n + 1))
                dots(n, n, 0, a, dots0_done, s0_ready)

            def copy_s(n, g, p, l):
                if l == 0:
                    dve.wait_ge(s0_ready, n + 1)
                else:
                    dve.wait_ge(s_ready, n - ITEMS + 1)
                after(dve, t_ready, GPI * (n - 1))
                nc.vector.tensor_scalar(ssc[:, p, :], sij[:, g, :], 1.0, None, ALU.mult).then_inc(s_copied, 1)

            def scores(n, g, p):
                dve.wait_ge(sjb_ready, n + 1)
                after(dve, exp_done, GPI * n)
                for q in range(GPI):
                    nc.vector.scalar_tensor_tensor(
                        out=t[:, q, :], in0=T[:, 0, q * P:(q + 1) * P], scalar=ssc[:, p, q:q + 1],
                        in1=masked[:, g, q, :], op0=ALU.add, op1=ALU.add).then_inc(t_ready, 1)
                dve.wait_ge(t_ready, GPI * (n + 1))
                nc.vector.scalar_tensor_tensor(out=t[:, :, :], in0=t[:, :, :], scalar=SLOPE, in1=t[:, :, :],
                                               op0=ALU.mult, op1=ALU.max).then_inc(max_steps, 1)
                dve.wait_ge(max_steps, 3 * n + 1)
                nc.vector.tensor_reduce(tmax[:, :], t[:, :, :], AX_X, ALU.max).then_inc(max_steps, 1)
                dve.wait_ge(max_steps, 3 * n + 2)
                nc.vector.tensor_scalar(negm[:, :], tmax[:, :], -1.0, None, ALU.mult).then_inc(max_steps, 1)

            def reciprocal(n):
                dve.wait_ge(exp_done, GPI * (n + 1))
                nc.vector.reciprocal(rden[:, :], den[:, :]).then_inc(rden_ready, 1)

            def residual(n, g):
                dve.wait_ge(rden_ready, n + 1)
                after(dve, ht_psum, KD * n)
                for q in range(GPI):
                    dve.wait_ge(agg_ready, BANKS * n + q // PER + 1)
                    nc.vector.scalar_tensor_tensor(
                        out=r[:, q, :], in0=T[:, q // PER, (q % PER) * D:(q % PER + 1) * D],
                        scalar=rden[:, q:q + 1], in1=xs[:, g, q, :], op0=ALU.mult, op1=ALU.add).then_inc(r_done, 1)

            def statistics1(n):
                for q in range(GPI):
                    dve.wait_ge(r_done, GPI * n + q + 1)
                    nc.vector.bn_stats(st1[:, q, :], r[:, q, :]).then_inc(bn1, 1)

            def aggregate1(n):
                for q in range(GPI):
                    nc.vector.bn_aggr(mv1[:, q, :], st1[:, q, :]).then_inc(mv1_done, 1)

            def normalise1(n):
                dve.wait_ge(rs1_steps, 2 * n + 2)
                for q in range(GPI):
                    nc.vector.tensor_scalar(r[:, q, :], r[:, q, :], mv1[:, q, 0:1], rs1[:, q:q + 1],
                                            ALU.subtract, ALU.mult).then_inc(n1_done, 1)

            def split_g(n, c):
                m = KH * n + c
                dve.wait_ge(gelu_done, 2 * m + 2)
                after(dve, w2_done, m - 3)
                nc.vector.tensor_tensor(Glo[c % 4][:, :], G[:, c % 2, :], Ghi[c % 4][:, :].bitcast(F32),
                                        ALU.subtract).then_inc(glo_ready, 1)

            def f_of(p, q):
                return F[:, p, q // PER, (q % PER) * D:(q % PER + 1) * D]

            def statistics2(n, p):
                dve.wait_ge(w2_done, KH * (n + 1))
                for q in range(GPI):
                    nc.vector.bn_stats(st2[:, q, :], f_of(p, q)).then_inc(bn2, 1)

            def aggregate2(n):
                for q in range(GPI):
                    nc.vector.bn_aggr(mv2[:, q, :], st2[:, q, :]).then_inc(mv2_done, 1)

            def centre2(n, g, p, l):
                for q in range(GPI):
                    dve.wait_ge(mv2_done, GPI * n + q + 1)
                    nc.vector.scalar_tensor_tensor(out=xs[:, g, q, :], in0=f_of(p, q), scalar=mv2[:, q, 0:1],
                                                   in1=g2r[:, l, :], op0=ALU.subtract, op1=ALU.mult).then_inc(f_free, 1)

            def finish2(n, g, l):
                dve.wait_ge(rs2_steps, 2 * n + 2)
                for q in range(GPI):
                    dve.wait_ge(f_free, GPI * n + q + 1)
                    nc.vector.scalar_tensor_tensor(out=xs[:, g, q, :], in0=xs[:, g, q, :], scalar=rs2[:, q:q + 1],
                                                   in1=be2r[:, l, :], op0=ALU.mult, op1=ALU.add).then_inc(x_done, 1)

            def next_dots(n, g, l, a):
                if l + 1 < L:
                    dve.wait_ge(x_done, GPI * (n + 1))
                    dots(n, g, l + 1, a, dots_done, s_ready)

            features(0)
            dve.wait_ge(s_const, 16 * CONSTS)
            first_dots(0, 0)
            first_dots(0, 1)
            copy_s(0, 0, 0, 0)
            scores(0, 0, 0)
            features(1)
            reciprocal(0)
            residual(0, 0)
            statistics1(0)
            dve.wait_ge(bn1, GPI)
            aggregate1(0)
            first_dots(1, 0)
            first_dots(1, 1)
            copy_s(1, 1, 1, 0)
            normalise1(0)
            dve.wait_ge(s_const2, 16 * CONSTS2)
            nc.vector.tensor_tensor(beb2[:, :, :], be1c[:, :, :], b2c[:, :, :], ALU.add).then_inc(beb2_ready, 1)
            features(2)
            scores(1, 1, 1)
            first_dots(2, 0)

            def body(l, i, p):
                n, nxt, far, prev = at(l, i, 0), at(l, i, 1), at(l, i, 2), at(l, i, -1)
                feat = i + 3 if has_features(l, i) else None
                first_far = l == 0 and (not isinstance(i, int) or i + 2 < ITEMS)
                for c in range(KH):
                    if c == 2 and nxt is not None:
                        dve.wait_ge(bn1, GPI * (nxt + 1))
                    if c == 4 and feat is not None:
                        dve.wait_ge(in_bn, GPI * (feat + 1))
                    if c == 4 and prev is not None:
                        dve.wait_ge(bn2, GPI * (prev + 1))
                    split_g(n, c)
                    if c == 0:
                        if nxt is not None:
                            reciprocal(nxt)
                        if first_far:
                            first_dots(far, 1)
                    if c == 1:
                        if far is not None:
                            copy_s(far, group(l, i, 2), p, 0 if first_far else 1)
                        if nxt is not None:
                            residual(nxt, group(l, i, 1))
                            statistics1(nxt)
                    if c == 2:
                        if nxt is not None:
                            aggregate1(nxt)
                        if prev is not None:
                            statistics2(prev, 1 - p)
                        if nxt is not None:
                            normalise1(nxt)
                    if c == 3:
                        if far is not None:
                            scores(far, group(l, i, 2), p)
                        if feat is not None:
                            statistics0(feat)
                    if c == 4:
                        if feat is not None:
                            aggregate0(feat)
                        if prev is not None:
                            aggregate2(prev)
                            centre2(prev, group(l, i, -1), 1 - p, layer(l, i, -1))
                    if c == 5:
                        if feat is not None:
                            minus_mean(feat)
                        if prev is not None:
                            finish2(prev, group(l, i, -1), layer(l, i, -1))
                        if feat is not None:
                            mask(feat)
                    if c == 6:
                        if prev is not None:
                            next_dots(prev, group(l, i, -1), layer(l, i, -1), 0)
                        if feat is not None:
                            scale_mask(feat)
                    if c == 7:
                        if prev is not None:
                            next_dots(prev, group(l, i, -1), layer(l, i, -1), 1)
                        if feat is not None:
                            first_dots(feat, 0)

            steps(dve, body)
            last = STEPS - 1
            statistics2(last, last % 2)
            dve.wait_ge(bn2, GPI * STEPS)
            aggregate2(last)
            centre2(last, ITEMS - 1, last % 2, L - 1)
            finish2(last, ITEMS - 1, L - 1)

        @block.tensor
        def _(pe):
            def sj_rows(n, p):
                pe.wait_ge(s_copied, n + 1)
                for q in range(GPI):
                    last = nc.tensor.transpose(T[:, 0, q * P:(q + 1) * P],
                                               ssc[:, p, GPI + q:GPI + q + 1].to_broadcast([P, P]), ident[:, :])
                last.then_inc(sjb_ready, 1)

            def transpose_e(n):
                pe.wait_ge(exp_done, GPI * (n + 1))
                after(pe, h_b2, KD * n)
                for q in range(GPI):
                    last = nc.tensor.transpose(T[:, 1, q * P:(q + 1) * P], e[:, q, :], ident[:, :])
                last.then_inc(et_ready, 1)

            def aggregate(n, g):
                pe.wait_ge(et_copied, n + 1)
                for q in range(GPI):
                    last = nc.tensor.matmul(T[:, q // PER, (q % PER) * D:(q % PER + 1) * D], eT[:, q, :],
                                            xs[:, g, q, :], start=True, stop=True, skip_group_check=True)
                    if q % PER == PER - 1:
                        last.then_inc(agg_ready, 1)

            def transpose_h(n):
                pe.wait_ge(n1_done, GPI * (n + 1))
                for k in range(KD):
                    for q in range(GPI):
                        last = nc.tensor.transpose(T[:, k, q * P:(q + 1) * P], r[:, q, k * P:(k + 1) * P], ident[:, :])
                    last.then_inc(ht_psum, 1)

            def w1(n, p, l, c, first):
                m = KH * n + c
                if first:
                    pe.wait_ge(w1_ready, KH * l + c + 1)
                if c == 0:
                    pe.wait_ge(h_act, 2 * KD * (n + 1))
                    pe.wait_ge(h_lo, KD * (n + 1))
                after(pe, gelu_done, 2 * (m - 1))
                cols = slice(c * P, (c + 1) * P)
                pairs = [(w, h, k) for w, h in ((W1hi, Hhi[p]), (W1hi, Hlo[p]), (W1lo, Hhi[p])) for k in range(KD)]
                for at_, (w, h, k) in enumerate(pairs):
                    last = nc.tensor.matmul(U[:, c % 2, :], w[:, k, cols], h[:, k, :],
                                            start=(at_ == 0), stop=(at_ == len(pairs) - 1))
                last.then_inc(u_ready, 1)

            def open_f(n, p):
                pe.wait_ge(h_b2, KD * (n + 1))
                after(pe, f_free, GPI * (n - 1))
                for q in range(GPI):
                    for k in range(KD):
                        c0 = (q % PER) * D + k * P
                        last = nc.tensor.matmul(F[:, p, q // PER, c0:c0 + P], hTb[:, k, q * P:(q + 1) * P], ident[:, :],
                                                is_transpose=True, start=(q % PER == 0 and k == 0), stop=False,
                                                skip_group_check=True)
                last.then_inc(f_open, 1)

            def w2(n, p, l, c, first):
                m = KH * n + c
                if first:
                    pe.wait_ge(w2_ready, KH * l + (c + 1 if c < KH - LAG - 1 else KH))
                pe.wait_ge(gelu_done, 2 * m + 2)
                pe.wait_ge(glo_ready, m + 1)
                for q in range(GPI):
                    toks = slice(q * P, (q + 1) * P)
                    dst = F[:, p, q // PER, (q % PER) * D:(q % PER + 1) * D]
                    for g, w in ((Ghi[c % 4], W2hi), (Ghi[c % 4], W2lo), (Glo[c % 4], W2hi)):
                        last = nc.tensor.matmul(dst, g[:, toks], w[:, c, :], start=False, stop=(c == KH - 1),
                                                skip_group_check=True)
                last.then_inc(w2_done, 1)

            pe.wait_ge(s_id, 4)
            sj_rows(0, 0)
            transpose_e(0)
            aggregate(0, 0)
            transpose_h(0)
            pe.wait_ge(h_b2, 1)
            sj_rows(1, 1)

            def body(l, i, p):
                n, nxt, far, prev = at(l, i, 0), at(l, i, 1), at(l, i, 2), at(l, i, -1)
                first = isinstance(i, int) and i == 0
                for c in range(KH):
                    w1(n, p, l, c, first)
                    if c < LAG:
                        if prev is not None:
                            w2(prev, 1 - p, layer(l, i, -1), KH - LAG + c, False)
                    else:
                        if c == LAG:
                            open_f(n, p)
                        w2(n, p, l, c - LAG, first)
                    if c == 0 and nxt is not None:
                        transpose_e(nxt)
                    if c == 1 and nxt is not None:
                        aggregate(nxt, group(l, i, 1))
                    if c == 2 and far is not None:
                        pe.wait_ge(r_done, GPI * (far - 1) + PER)
                        sj_rows(far, p)
                    if c == 4 and nxt is not None:
                        if far is not None:
                            pe.wait_ge(t_ready, GPI * (far + 1))
                        transpose_h(nxt)

            steps(pe, body)
            for c in range(KH - LAG, KH):
                w2(STEPS - 1, (STEPS - 1) % 2, L - 1, c, False)


_INS = ['x', 'adj', 'L0_gnn_attn_w', 'L0_gnn_attn_b', 'L0_gnn_W1', 'L0_gnn_b1', 'L0_gnn_W2', 'L0_gnn_b2',
        'L0_gnn_g1', 'L0_gnn_beta1', 'L0_gnn_g2', 'L0_gnn_beta2']
_OUTS = [((64, 128, 256), 'float32')]


def kernel(**inputs):
    import numpy as _np
    import concourse.bacc as _bacc
    from concourse import mybir as _mybir
    from concourse.bass_utils import run_bass_kernel_spmd as _run

    nc = _bacc.Bacc("TRN2", target_bir_lowering=False, num_devices=1)
    arrays, args = {}, []
    for name in _INS:
        a = _np.ascontiguousarray(inputs[name])
        arrays[f"in_{name}_dram"] = a
        args.append(nc.dram_tensor(f"in_{name}_dram", a.shape, _mybir.dt.from_np(a.dtype), kind="ExternalInput").ap())
    for i, (shape, dtype) in enumerate(_OUTS):
        dt = _mybir.dt.from_np(_np.dtype(dtype))
        args.append(nc.dram_tensor(f"out_{i}_dram", shape, dt, kind="ExternalOutput").ap())
    gnn_kernel(nc, *args)
    r = _run(nc, [arrays], core_ids=[0])
    return r.results[0]["out_0_dram"]
```

```python
from contextlib import ExitStack

import concourse.bass as bass
from concourse import mybir
from concourse.alu_op_type import AluOpType as ALU

ACT = mybir.ActivationFunctionType
AX_X = mybir.AxisListType.X
F32 = mybir.dt.float32
F32R = mybir.dt.float32r
BF16 = mybir.dt.bfloat16
I32 = mybir.dt.int32

P = 128
GPI = 4
TOK = GPI * P
EPS = 1e-5
SLOPE = 0.2
BIG = 3.0e38
POOL_CHUNKS = (0, 7)
LAG = 2


def gnn_kernel(nc, x, adj, attn_w, attn_b, W1, b1, W2, b2, g1, beta1, g2, beta2, out):
    B, N, D = x.shape
    L, _, HID = W1.shape
    assert N == P and D % P == 0 and HID % P == 0 and B % GPI == 0
    ITEMS = B // GPI
    KD = D // P
    KH = HID // P
    BANKS = GPI * D // 512
    PER = GPI // BANKS
    STEPS = L * ITEMS
    assert KH == 8 and ITEMS % 2 == 0 and BANKS == 2 and KD == 2 and GPI * P == 512

    with ExitStack() as ctx:
        def sb(name, shape, dt=F32):
            return ctx.enter_context(nc.sbuf_tensor(name, shape, dt))

        def ps(name, shape):
            return ctx.enter_context(nc.psum_tensor(name, shape, F32))

        def sem(name):
            return ctx.enter_context(nc.semaphore(name))

        xs = sb("xs", [P, ITEMS, GPI, D])
        masked = sb("masked", [P, ITEMS, GPI, P], BF16)
        sij = sb("sij", [P, ITEMS, 2 * GPI])
        W1hi = sb("W1hi", [P, KD, HID], F32R)
        W1lo = sb("W1lo", [P, KD, HID], F32R)
        W2hi = sb("W2hi", [P, KH, D], F32R)
        W2lo = sb("W2lo", [P, KH, D], F32R)
        W1raw = sb("W1raw", [P, KD, HID])
        W2raw = sb("W2raw", [P, KH, D])
        aw = sb("aw", [P, L, 2, D])
        ab = sb("ab", [P, L])
        g2r = sb("g2r", [P, L, D])
        be2r = sb("be2r", [P, L, D])
        b1c = sb("b1c", [P, L, KH])
        g1c = sb("g1c", [P, L, KD])
        be1c = sb("be1c", [P, L, KD])
        b2c = sb("b2c", [P, L, KD])
        ident = sb("ident", [P, P])
        xin = sb("xin", [P, GPI, D])
        adjin = sb("adjin", [P, GPI, P], I32)
        ssc = sb("ssc", [P, 2, 2 * GPI])
        t = sb("t", [P, P, GPI])
        e = sb("e", [P, GPI, P])
        eT = sb("eT", [P, GPI, P])
        tmax = sb("tmax", [P, GPI])
        negm = sb("negm", [P, GPI])
        den = sb("den", [P, GPI])
        rden = sb("rden", [P, GPI])
        r = sb("r", [P, GPI, D])
        hT = [sb(f"hT{b}", [P, KD, TOK]) for b in range(2)]
        rT = sb("rT", [P, KD, TOK])
        Hhi = [sb(f"Hhi{b}", [P, KD, TOK], F32R) for b in range(2)]
        Hlo = [sb(f"Hlo{b}", [P, KD, TOK], F32R) for b in range(2)]
        G = sb("G", [P, 2, TOK])
        Ghi = [sb(f"Ghi{b}", [P, TOK], F32R) for b in range(4)]
        Glo = [sb(f"Glo{b}", [P, TOK], F32R) for b in range(4)]
        junk = sb("junk", [P, 2, D], BF16)
        st0 = sb("st0", [P, GPI, 6])
        st1 = sb("st1", [P, GPI, 6])
        st2 = sb("st2", [P, GPI, 6])
        mv0 = sb("mv0", [P, GPI, 2])
        mv1 = sb("mv1", [P, GPI, 2])
        mv2 = sb("mv2", [P, GPI, 2])
        ve0 = sb("ve0", [P, GPI])
        ve1 = sb("ve1", [P, GPI])
        ve2 = sb("ve2", [P, GPI])
        rs0 = sb("rs0", [P, GPI])
        rs1 = sb("rs1", [P, GPI])
        rs2 = sb("rs2", [P, GPI])
        nmr = sb("nmr", [P, GPI])
        nm1 = sb("nm1", [P, GPI])
        nmr1 = sb("nmr1", [P, GPI])
        mhalf = sb("mhalf", [P, GPI])
        mone = sb("mone", [P, GPI])
        epsc = sb("epsc", [P, GPI])

        U = ps("U", [P, 2, 512])
        FT = ps("FT", [P, KD, 512])
        F = ps("F", [P, BANKS, 512])
        T = ps("T", [P, 2, 512])

        s_const = sem("s_const")
        s_const2 = sem("s_const2")
        s_w1raw = sem("s_w1raw")
        s_w2raw = sem("s_w2raw")
        s_xin = sem("s_xin")
        s_adj = sem("s_adj")
        s_out = sem("s_out")
        s_id = sem("s_id")
        w1_ready = sem("w1_ready")
        w2_ready = sem("w2_ready")
        w1_hi = sem("w1_hi")
        w2_hi = sem("w2_hi")
        in_bn = sem("in_bn")
        in_mv = sem("in_mv")
        in_rs = sem("in_rs")
        in_nmr = sem("in_nmr")
        x0_done = sem("x0_done")
        mask_done = sem("mask_done")
        mask_ready = sem("mask_ready")
        dots0_done = sem("dots0_done")
        dots_done = sem("dots_done")
        s0_ready = sem("s0_ready")
        s_ready = sem("s_ready")
        s_copied = sem("s_copied")
        sjb_ready = sem("sjb_ready")
        sj_stored = sem("sj_stored")
        sj_loaded = sem("sj_loaded")
        t_ready = sem("t_ready")
        max_steps = sem("max_steps")
        exp_done = sem("exp_done")
        et_ready = sem("et_ready")
        et_copied = sem("et_copied")
        rden_ready = sem("rden_ready")
        agg_ready = sem("agg_ready")
        r_done = sem("r_done")
        bn1 = sem("bn1")
        mv1_done = sem("mv1_done")
        rs1_steps = sem("rs1_steps")
        n1_done = sem("n1_done")
        ht_psum = sem("ht_psum")
        h_act = sem("h_act")
        h_lo = sem("h_lo")
        u_ready = sem("u_ready")
        gelu_done = sem("gelu_done")
        glo_ready = sem("glo_ready")
        glo_pool = sem("glo_pool")
        w2_done = sem("w2_done")
        ft0_ready = sem("ft0_ready")
        ft_read = sem("ft_read")
        back_ready = sem("back_ready")
        bn2 = sem("bn2")
        mv2_done = sem("mv2_done")
        f_free = sem("f_free")
        rs2_steps = sem("rs2_steps")
        x_done = sem("x_done")
        o_ready = sem("o_ready")
        o_last = sem("o_last")

        x_g = x.rearrange("(i q) n d -> i n q d", q=GPI)
        out_g = out.rearrange("(i q) n d -> i n q d", q=GPI)
        adj_g = adj.rearrange("(i q) n m -> i n q m", q=GPI)
        CONSTS, CONSTS2 = 2, 6
        sj_dram = nc.dram_tensor("sj_dram", [P, GPI], F32, kind="Internal").ap()

        def steps(engine, body):
            for l in range(L):
                head = 3 if l == 0 else 1
                tail = ITEMS - 3 if l in (0, L - 1) else ITEMS - 1
                for i in range(head):
                    body(l, i, i % 2)
                with engine.Fori(0, (tail - head) // 2) as j:
                    body(l, 2 * j + head, 1)
                    body(l, 2 * j + head + 1, 0)
                for i in range(tail, ITEMS):
                    body(l, i, i % 2)

        def at(l, i, off):
            n = l * ITEMS + i + off
            if isinstance(n, int) and not 0 <= n < STEPS:
                return None
            return n

        def group(l, i, off):
            if isinstance(i, int):
                return (i + off) % ITEMS
            return i + off if off < 2 else (i + off) % ITEMS

        def layer(l, i, off):
            return (l * ITEMS + i + off) // ITEMS if isinstance(i, int) else l

        def has_features(l, i):
            return l == 0 and (not isinstance(i, int) or i + 3 < ITEMS)

        def first_scores(l, i):
            return l == 0 and (not isinstance(i, int) or i + 2 < ITEMS)

        def last_of_layer(l, i):
            return isinstance(i, int) and i == ITEMS - 1 and l < L - 1

        def after(engine, semaphore, value):
            if not isinstance(value, int) or value > 0:
                engine.wait_ge(semaphore, value)

        def wait_glo(engine, n, c):
            if c in POOL_CHUNKS:
                engine.wait_ge(glo_pool, 2 * n + POOL_CHUNKS.index(c) + 1)
            else:
                engine.wait_ge(glo_ready, (KH - 2) * n + c)

        block = ctx.enter_context(nc.Block())

        @block.sync
        def _(sp):
            def load(n):
                if not (isinstance(n, int) and n == 0):
                    sp.wait_ge(x0_done, GPI * n)
                    sp.wait_ge(mask_done, n)
                sp.dma_start(xin[:, :, :], x_g[n, :, :, :]).then_inc(s_xin, 16)
                sp.dma_start(adjin[:, :, :], adj_g[n, :, :, :]).then_inc(s_adj, 16)

            load(0)
            sp.dma_start(aw[:, :, :, :].rearrange("p l a d -> p (l a d)"),
                         attn_w.rearrange("l a -> (l a)").partition_broadcast(P)).then_inc(s_const, 16)
            sp.dma_start(ab[:, :], attn_b.partition_broadcast(P)).then_inc(s_const, 16)
            sp.dma_start(W1raw[:, :, :], W1[0].rearrange("(k p) f -> p k f", p=P)).then_inc(s_w1raw, 16)
            sp.dma_start(W2raw[:, :, :], W2[0].rearrange("(c p) d -> p c d", p=P)).then_inc(s_w2raw, 16)
            load(1)
            for dst, src in ((g1c, g1), (be1c, beta1), (b2c, b2), (b1c, b1)):
                sp.dma_start(dst[:, :, :], src.rearrange("l (k p) -> p l k", p=P),
                             allow_slow_non_contiguous=True).then_inc(s_const2, 16)
            for dst, src in ((g2r, g2), (be2r, beta2)):
                sp.dma_start(dst[:, :, :].rearrange("p l d -> p (l d)"),
                             src.rearrange("l d -> (l d)").partition_broadcast(P)).then_inc(s_const2, 16)
            with sp.Fori(2, ITEMS) as n:
                load(n)

            def load_weights(l):
                sp.wait_ge(w1_ready, KH * l)
                sp.wait_ge(w2_ready, KH * l)
                sp.dma_start(W1raw[:, :, :], W1[l].rearrange("(k p) f -> p k f", p=P)).then_inc(s_w1raw, 16)
                sp.dma_start(W2raw[:, :, :], W2[l].rearrange("(c p) d -> p c d", p=P)).then_inc(s_w2raw, 16)

            for l in range(1, L):
                load_weights(l)
            sp.wait_ge(x0_done, GPI * ITEMS)
            sp.dma_start(xin[:, :, :], x_g[0, :, :, :]).then_inc(s_xin, 16)
            with sp.Fori(0, ITEMS - 1) as g:
                sp.wait_ge(o_ready, g + 1)
                sp.dma_start(xin[:, :, :], x_g[g + 1, :, :, :]).then_inc(s_xin, 16)
                sp.dma_start(out_g[g, :, :, :], xs[:, g, :, :]).then_inc(s_out, 16)
            for q in range(GPI):
                sp.wait_ge(o_last, q + 1)
                sp.dma_start(out_g[ITEMS - 1, :, q, :], xs[:, ITEMS - 1, q, :]).then_inc(s_out, 16)
            sp.wait_ge(s_out, 16 * (ITEMS - 1 + GPI))

        @block.gpsimd
        def _(pool):
            nc.gpsimd.memset(ident[:, :], 0.0).then_inc(s_id, 1)
            nc.gpsimd.memset(mhalf[:, :], -0.5).then_inc(s_id, 1)
            nc.gpsimd.memset(epsc[:, :], EPS).then_inc(s_id, 1)
            nc.gpsimd.memset(mone[:, :], -1.0).then_inc(s_id, 1)
            pool.wait_ge(s_id, 4)
            nc.gpsimd.affine_select(out=ident[:, :], in_=ident[:, :], compare_op=ALU.not_equal, fill=1.0,
                                    base=0, pattern=[[-1, P]], channel_multiplier=1).then_inc(s_id, 1)

            def rstd(n, mv, mv_done, ve, rs, steps_sem):
                pool.wait_ge(mv_done, GPI * (n + 1))
                nc.gpsimd.tensor_tensor(ve[:, :], mv[:, :, 1], epsc[:, :], ALU.add).then_inc(steps_sem, 1)
                pool.wait_ge(steps_sem, 2 * n + 1)
                nc.gpsimd.tensor_tensor(rs[:, :], ve[:, :], mhalf[:, :], ALU.pow).then_inc(steps_sem, 1)

            def rstd1(n):
                pool.wait_ge(mv1_done, GPI * (n + 1))
                after(pool, n1_done, GPI * n)
                nc.gpsimd.tensor_tensor(ve1[:, :], mv1[:, :, 1], epsc[:, :], ALU.add).then_inc(rs1_steps, 1)
                nc.gpsimd.tensor_tensor(nm1[:, :], mv1[:, :, 0], mone[:, :], ALU.mult).then_inc(rs1_steps, 1)
                pool.wait_ge(rs1_steps, 4 * n + 2)
                nc.gpsimd.tensor_tensor(rs1[:, :], ve1[:, :], mhalf[:, :], ALU.pow).then_inc(rs1_steps, 1)
                pool.wait_ge(rs1_steps, 4 * n + 3)
                nc.gpsimd.tensor_tensor(nmr1[:, :], nm1[:, :], rs1[:, :], ALU.mult).then_inc(rs1_steps, 1)

            def w1_lo(l, c0, c1):
                pool.wait_ge(w1_hi, KH * l + c1)
                cols = slice(c0 * P, c1 * P)
                nc.gpsimd.tensor_tensor(W1lo[:, :, cols], W1raw[:, :, cols], W1hi[:, :, cols].bitcast(F32),
                                        ALU.subtract).then_inc(w1_ready, c1 - c0)

            def w2_lo(l, c0, c1):
                pool.wait_ge(w2_hi, KH * l + c1)
                nc.gpsimd.tensor_tensor(W2lo[:, c0:c1, :], W2raw[:, c0:c1, :], W2hi[:, c0:c1, :].bitcast(F32),
                                        ALU.subtract).then_inc(w2_ready, c1 - c0)

            def split_h(n, p):
                after(pool, u_ready, KH * (n - 1))
                for k in range(KD):
                    pool.wait_ge(h_act, 2 * (KD * n + k) + 2)
                    nc.gpsimd.tensor_tensor(Hlo[p][:, k, :], hT[p][:, k, :], Hhi[p][:, k, :].bitcast(F32),
                                            ALU.subtract).then_inc(h_lo, 1)

            def split_g(n, c):
                pool.wait_ge(gelu_done, 2 * (KH * n + c) + 2)
                nc.gpsimd.tensor_tensor(Glo[c % 4][:, :], G[:, c % 2, :], Ghi[c % 4][:, :].bitcast(F32),
                                        ALU.subtract).then_inc(glo_pool, 1)

            rstd(0, mv0, in_mv, ve0, rs0, in_rs)
            w1_lo(0, 0, KH)
            rstd(1, mv0, in_mv, ve0, rs0, in_rs)
            w2_lo(0, 0, 3)
            rstd1(0)
            rstd(2, mv0, in_mv, ve0, rs0, in_rs)
            split_h(0, 0)
            w2_lo(0, 3, KH)

            def output(n, g):
                pool.wait_ge(x_done, GPI * (n + 1))
                pool.wait_ge(s_xin, 16 * (ITEMS + g + 1))
                nc.gpsimd.tensor_tensor(xs[:, g, :, :], xs[:, g, :, :], xin[:, :, :], ALU.add).then_inc(o_ready, 1)

            def body(l, i, p):
                nxt, prev = at(l, i, 1), at(l, i, -1)
                split_g(at(l, i, 0), 0)
                if nxt is not None:
                    rstd1(nxt)
                if last_of_layer(l, i):
                    w1_lo(l + 1, 0, 3)
                if l > 0 and isinstance(i, int) and i == 0:
                    w1_lo(l, 6, KH)
                    w2_lo(l, 4, KH)
                if has_features(l, i):
                    rstd(i + 3, mv0, in_mv, ve0, rs0, in_rs)
                if prev is not None:
                    rstd(prev, mv2, mv2_done, ve2, rs2, rs2_steps)
                if nxt is not None:
                    split_h(nxt, 1 - p)
                if last_of_layer(l, i):
                    w1_lo(l + 1, 3, 6)
                split_g(at(l, i, 0), KH - 1)
                if last_of_layer(l, i):
                    w2_lo(l + 1, 0, 4)
                if prev is not None and layer(l, i, -1) == L - 1:
                    output(prev, group(l, i, -1))

            steps(pool, body)
            rstd(STEPS - 1, mv2, mv2_done, ve2, rs2, rs2_steps)

        @block.scalar
        def _(act):
            def features(n):
                act.wait_ge(in_nmr, n + 1)
                for q in range(GPI):
                    nc.scalar.activation(xs[:, n, q, :], xin[:, q, :], ACT.Relu, bias=nmr[:, q:q + 1],
                                         scale=rs0[:, q:q + 1]).then_inc(x0_done, 1)

            def exps(n):
                act.wait_ge(max_steps, 3 * (n + 1))
                after(act, et_ready, n)
                after(act, rden_ready, n)
                for q in range(GPI):
                    nc.scalar.activation(e[:, q, :], t[:, :, q], ACT.Exp, bias=negm[:, q:q + 1],
                                         accum_out=den[:, q:q + 1]).then_inc(exp_done, 1)

            def store_sj(n, g, l):
                if l == 0:
                    act.wait_ge(s0_ready, n + 1)
                else:
                    act.wait_ge(s_ready, n - ITEMS + 1)
                after(act, sj_loaded, 16 * (n - 2))
                nc.scalar.dma_start(sj_dram, sij[:, g, GPI:2 * GPI]).then_inc(sj_stored, 16)

            def load_sj(n):
                act.wait_ge(sj_stored, 16 * (n - 1))
                act.wait_ge(exp_done, GPI * n)
                nc.scalar.dma_start(t[:, :, :].rearrange("p j q -> p (j q)"),
                                    sj_dram.rearrange("j q -> (j q)").partition_broadcast(P)).then_inc(sj_loaded, 16)

            def copy_eT(n):
                act.wait_ge(et_ready, n + 1)
                after(act, agg_ready, BANKS * n)
                nc.scalar.copy(eT[:, :, :], T[:, 1, :].rearrange("p (q j) -> p q j", q=GPI)).then_inc(et_copied, 1)

            def normalise1(n):
                act.wait_ge(rs1_steps, 4 * n + 4)
                for q in range(GPI):
                    nc.scalar.activation(r[:, q, :], r[:, q, :], ACT.Identity, bias=nmr1[:, q:q + 1],
                                         scale=rs1[:, q:q + 1]).then_inc(n1_done, 1)

            def affine_h(n, l, p):
                after(act, ft_read, KD * (n - 1))
                after(act, u_ready, KH * (n - 1))
                for k in range(KD):
                    act.wait_ge(ht_psum, KD * n + k + 1)
                    for dst in (hT[p], Hhi[p]):
                        nc.scalar.activation(dst[:, k, :], T[:, k, :], ACT.Identity, bias=be1c[:, l, k:k + 1],
                                             scale=g1c[:, l, k:k + 1]).then_inc(h_act, 1)

            def w1_hi_part(l, c0, c1):
                act.wait_ge(s_w1raw, 16 * (l + 1))
                if l:
                    act.wait_ge(u_ready, KH * (ITEMS * l - 1) + c1)
                cols = slice(c0 * P, c1 * P)
                nc.scalar.copy(W1hi[:, :, cols], W1raw[:, :, cols]).then_inc(w1_hi, c1 - c0)

            def w2_hi_part(l, c0, c1):
                act.wait_ge(s_w2raw, 16 * (l + 1))
                if l:
                    act.wait_ge(w2_done, KH * (ITEMS * l - 1) + c1)
                nc.scalar.copy(W2hi[:, c0:c1, :], W2raw[:, c0:c1, :]).then_inc(w2_hi, c1 - c0)

            def gelu(n, l, c):
                m = KH * n + c
                act.wait_ge(u_ready, m + 1)
                if c >= 2:
                    wait_glo(act, n, c - 2)
                elif not isinstance(n, int) or n > 0:
                    wait_glo(act, n - 1, KH + c - 2)
                nc.scalar.activation(G[:, c % 2, :], U[:, c % 2, :], ACT.Gelu, bias=b1c[:, l, c:c + 1]).then_inc(gelu_done, 1)
                after(act, w2_done, m - 3)
                nc.scalar.activation(Ghi[c % 4][:, :], U[:, c % 2, :], ACT.Gelu, bias=b1c[:, l, c:c + 1]).then_inc(gelu_done, 1)

            features(0)
            w1_hi_part(0, 0, KH)
            exps(0)
            copy_eT(0)
            features(1)
            w2_hi_part(0, 0, KH)
            normalise1(0)
            act.wait_ge(s_const2, 16 * CONSTS2)
            affine_h(0, 0, 0)
            features(2)
            exps(1)

            def body(l, i, p):
                if at(l, i, 1) is not None:
                    copy_eT(at(l, i, 1))
                for c in range(KH):
                    gelu(at(l, i, 0), l, c)
                    if c == 1 and at(l, i, 2) is not None:
                        store_sj(at(l, i, 2), group(l, i, 2),
                                 0 if first_scores(l, i) else 1)
                    if c == 3 and at(l, i, 2) is not None:
                        load_sj(at(l, i, 2))
                    if last_of_layer(l, i):
                        if c == 1:
                            w1_hi_part(l + 1, 0, 2)
                        if c == 2:
                            w1_hi_part(l + 1, 2, 3)
                        if c == 5:
                            w1_hi_part(l + 1, 3, 6)
                        if c == KH - 1:
                            w2_hi_part(l + 1, 0, 4)
                    if l > 0 and isinstance(i, int) and i == 0 and c == 2:
                        w1_hi_part(l, 6, KH)
                        w2_hi_part(l, 4, KH)
                    if c == 3 and at(l, i, 1) is not None:
                        normalise1(at(l, i, 1))
                    if c == 4 and at(l, i, 1) is not None:
                        affine_h(at(l, i, 1), layer(l, i, 1), 1 - p)
                    if c == 6 and at(l, i, 2) is not None:
                        exps(at(l, i, 2))
                    if c == 7 and has_features(l, i):
                        features(i + 3)

            steps(act, body)

        @block.vector
        def _(dve):
            dve.wait_ge(s_id, 5)

            def dots(m, g, l, start, pairs, done):
                for k, (q, a) in enumerate(pairs, start):
                    if k >= 2:
                        dve.wait_ge(done, 2 * GPI * m + k - 1)
                    nc.vector.scalar_tensor_tensor(
                        out=junk[:, k % 2, :], in0=xs[:, g, q, :], scalar=1.0, in1=aw[:, l, a, :], op0=ALU.mult,
                        op1=ALU.mult, accum_out=sij[:, g, a * GPI + q:a * GPI + q + 1]).then_inc(done, 1)

            def add_b(m, g, l, done, ready):
                dve.wait_ge(done, 2 * GPI * (m + 1))
                nc.vector.tensor_scalar(sij[:, g, 0:GPI], sij[:, g, 0:GPI], ab[:, l:l + 1], None,
                                        ALU.add).then_inc(ready, 1)

            def statistics0(n):
                dve.wait_ge(s_xin, 16 * (n + 1))
                for q in range(GPI):
                    nc.vector.bn_stats(st0[:, q, :], xin[:, q, :]).then_inc(in_bn, 1)

            def aggregate0(n):
                for q in range(GPI):
                    nc.vector.bn_aggr(mv0[:, q, :], st0[:, q, :]).then_inc(in_mv, 1)

            def minus_mean(n):
                dve.wait_ge(in_rs, 2 * n + 2)
                nc.vector.scalar_tensor_tensor(out=nmr[:, :], in0=mv0[:, :, 0], scalar=-1.0, in1=rs0[:, :],
                                               op0=ALU.mult, op1=ALU.mult).then_inc(in_nmr, 1)

            def mask(n):
                dve.wait_ge(s_adj, 16 * (n + 1))
                nc.vector.scalar_tensor_tensor(
                    out=masked[:, n, :, :], in0=adjin[:, :, :], scalar=-1.0,
                    in1=ident[:, :].unsqueeze(1).broadcast_to([P, GPI, P]), op0=ALU.mult,
                    op1=ALU.is_ge).then_inc(mask_done, 1)

            def scale_mask(n):
                dve.wait_ge(mask_done, n + 1)
                nc.vector.tensor_scalar(masked[:, n, :, :], masked[:, n, :, :], -BIG, None, ALU.mult).then_inc(mask_ready, 1)

            def features(n):
                statistics0(n)
                dve.wait_ge(in_bn, GPI * (n + 1))
                aggregate0(n)
                mask(n)
                minus_mean(n)
                scale_mask(n)

            def first_dots(n):
                for q in range(GPI):
                    dve.wait_ge(x0_done, GPI * n + q + 1)
                    dots(n, n, 0, 2 * q, [(q, 0), (q, 1)], dots0_done)
                add_b(n, n, 0, dots0_done, s0_ready)

            def copy_s(n, g, p, l):
                if l == 0:
                    dve.wait_ge(s0_ready, n + 1)
                else:
                    dve.wait_ge(s_ready, n - ITEMS + 1)
                after(dve, t_ready, GPI * (n - 1))
                nc.vector.tensor_scalar(ssc[:, p, :], sij[:, g, :], 1.0, None, ALU.mult).then_inc(s_copied, 1)

            def score_sums(n, g, p):
                dve.wait_ge(s_copied, n + 1)
                if isinstance(n, int) and n < 2:
                    dve.wait_ge(sjb_ready, n + 1)
                    after(dve, exp_done, GPI * n)
                else:
                    dve.wait_ge(sj_loaded, 16 * (n - 1))
                for q in range(GPI):
                    rows = T[:, 0, q * P:(q + 1) * P] if isinstance(n, int) and n < 2 else t[:, :, q]
                    nc.vector.scalar_tensor_tensor(
                        out=t[:, :, q], in0=rows, scalar=ssc[:, p, q:q + 1],
                        in1=masked[:, g, q, :], op0=ALU.add, op1=ALU.add).then_inc(t_ready, 1)

            def leaky(n):
                dve.wait_ge(t_ready, GPI * (n + 1))
                nc.vector.scalar_tensor_tensor(out=t[:, :, :], in0=t[:, :, :], scalar=SLOPE, in1=t[:, :, :],
                                               op0=ALU.mult, op1=ALU.max).then_inc(max_steps, 1)

            def row_max(n):
                dve.wait_ge(max_steps, 3 * n + 1)
                nc.vector.tensor_reduce(tmax[:, :], t[:, :, :].rearrange("p j q -> p q j"), AX_X, ALU.max).then_inc(max_steps, 1)

            def minus_max(n):
                dve.wait_ge(max_steps, 3 * n + 2)
                nc.vector.tensor_scalar(negm[:, :], tmax[:, :], -1.0, None, ALU.mult).then_inc(max_steps, 1)

            def reciprocal(n):
                dve.wait_ge(exp_done, GPI * (n + 1))
                nc.vector.reciprocal(rden[:, :], den[:, :]).then_inc(rden_ready, 1)

            def residual(n, g):
                dve.wait_ge(rden_ready, n + 1)
                after(dve, ht_psum, KD * n)
                for q in range(GPI):
                    dve.wait_ge(agg_ready, BANKS * n + q // PER + 1)
                    nc.vector.scalar_tensor_tensor(
                        out=r[:, q, :], in0=T[:, q // PER, (q % PER) * D:(q % PER + 1) * D],
                        scalar=rden[:, q:q + 1], in1=xs[:, g, q, :], op0=ALU.mult, op1=ALU.add).then_inc(r_done, 1)

            def statistics1(n):
                for q in range(GPI):
                    dve.wait_ge(r_done, GPI * n + q + 1)
                    nc.vector.bn_stats(st1[:, q, :], r[:, q, :]).then_inc(bn1, 1)

            def aggregate1(n):
                for q in range(GPI):
                    nc.vector.bn_aggr(mv1[:, q, :], st1[:, q, :]).then_inc(mv1_done, 1)

            def split_g(n, c):
                m = KH * n + c
                dve.wait_ge(gelu_done, 2 * m + 2)
                nc.vector.tensor_tensor(Glo[c % 4][:, :], G[:, c % 2, :], Ghi[c % 4][:, :].bitcast(F32),
                                        ALU.subtract).then_inc(glo_ready, 1)

            def f_of(q):
                return F[:, q // PER, (q % PER) * D:(q % PER + 1) * D]

            def residual2(n, p, l):
                after(dve, back_ready, BANKS * n)
                for k in range(KD):
                    if k == 0:
                        dve.wait_ge(ft0_ready, n + 1)
                    else:
                        dve.wait_ge(w2_done, KH * (n + 1))
                    nc.vector.scalar_tensor_tensor(out=rT[:, k, :], in0=FT[:, k, :], scalar=b2c[:, l, k:k + 1],
                                                   in1=hT[p][:, k, :], op0=ALU.add, op1=ALU.add).then_inc(ft_read, 1)

            def statistics2(n):
                for q in range(GPI):
                    dve.wait_ge(back_ready, BANKS * n + q // PER + 1)
                    nc.vector.bn_stats(st2[:, q, :], f_of(q)).then_inc(bn2, 1)

            def aggregate2(n):
                for q in range(GPI):
                    nc.vector.bn_aggr(mv2[:, q, :], st2[:, q, :]).then_inc(mv2_done, 1)

            def centre2(n, g, l):
                for q in range(GPI):
                    dve.wait_ge(mv2_done, GPI * n + q + 1)
                    nc.vector.scalar_tensor_tensor(out=xs[:, g, q, :], in0=f_of(q), scalar=mv2[:, q, 0:1],
                                                   in1=g2r[:, l, :], op0=ALU.subtract, op1=ALU.mult).then_inc(f_free, 1)

            def finish2(n, g, l):
                dve.wait_ge(rs2_steps, 2 * n + 2)
                for q in range(GPI):
                    dve.wait_ge(f_free, GPI * n + q + 1)
                    nc.vector.scalar_tensor_tensor(out=xs[:, g, q, :], in0=xs[:, g, q, :], scalar=rs2[:, q:q + 1],
                                                   in1=be2r[:, l, :], op0=ALU.mult, op1=ALU.add).then_inc(x_done, 1)

            def next_dots(n, g, l, a):
                if l + 1 < L:
                    dve.wait_ge(x_done, GPI * (n + 1))
                    dots(n, g, l + 1, a * GPI, [(q, a) for q in range(GPI)], dots_done)
                    if a == 1:
                        add_b(n, g, l + 1, dots_done, s_ready)

            features(0)
            dve.wait_ge(s_const, 16 * CONSTS)
            first_dots(0)
            copy_s(0, 0, 0, 0)
            score_sums(0, 0, 0)
            leaky(0)
            row_max(0)
            minus_max(0)
            features(1)
            reciprocal(0)
            residual(0, 0)
            statistics1(0)
            dve.wait_ge(bn1, GPI)
            aggregate1(0)
            first_dots(1)
            copy_s(1, 1, 1, 0)
            dve.wait_ge(s_const2, 16 * CONSTS2)
            features(2)
            score_sums(1, 1, 1)
            leaky(1)
            row_max(1)
            minus_max(1)
            first_dots(2)

            def body(l, i, p):
                n, nxt, far, prev = at(l, i, 0), at(l, i, 1), at(l, i, 2), at(l, i, -1)
                feat = i + 3 if has_features(l, i) else None
                for c in range(KH):
                    if c == 3 and feat is not None:
                        dve.wait_ge(in_bn, GPI * (feat + 1))
                    if c == 4 and prev is not None:
                        dve.wait_ge(bn2, GPI * (prev + 1))
                    if c == 1 and prev is not None:
                        residual2(prev, 1 - p, layer(l, i, -1))
                    if c == 1:
                        if far is not None:
                            copy_s(far, group(l, i, 2), p, 0 if first_scores(l, i) else 1)
                        if nxt is not None:
                            residual(nxt, group(l, i, 1))
                            statistics1(nxt)
                            dve.wait_ge(bn1, GPI * (nxt + 1))
                    if c not in POOL_CHUNKS:
                        split_g(n, c)
                    if c == 0 and nxt is not None:
                        reciprocal(nxt)
                    if c == 1 and nxt is not None:
                        aggregate1(nxt)
                    if c == 2:
                        if feat is not None:
                            statistics0(feat)
                    if c == 3:
                        if feat is not None:
                            aggregate0(feat)
                        if prev is not None:
                            statistics2(prev)
                        if far is not None:
                            score_sums(far, group(l, i, 2), p)
                    if c == 4:
                        if prev is not None:
                            aggregate2(prev)
                        if far is not None:
                            leaky(far)
                        if prev is not None:
                            centre2(prev, group(l, i, -1), layer(l, i, -1))
                        if far is not None:
                            row_max(far)
                        if feat is not None:
                            minus_mean(feat)
                    if c == 5:
                        if far is not None:
                            minus_max(far)
                        if prev is not None:
                            finish2(prev, group(l, i, -1), layer(l, i, -1))
                        if feat is not None:
                            mask(feat)
                    if c == 6:
                        if prev is not None:
                            next_dots(prev, group(l, i, -1), layer(l, i, -1), 0)
                        if feat is not None:
                            scale_mask(feat)
                        if prev is not None:
                            next_dots(prev, group(l, i, -1), layer(l, i, -1), 1)
                    if c == 7 and feat is not None:
                        first_dots(feat)

            steps(dve, body)
            last = STEPS - 1
            residual2(last, last % 2, L - 1)
            statistics2(last)
            dve.wait_ge(bn2, GPI * STEPS)
            aggregate2(last)
            centre2(last, ITEMS - 1, L - 1)
            finish2(last, ITEMS - 1, L - 1)
            dve.wait_ge(s_xin, 16 * 2 * ITEMS)
            for q in range(GPI):
                dve.wait_ge(x_done, GPI * last + q + 1)
                nc.vector.tensor_tensor(xs[:, ITEMS - 1, q, :], xs[:, ITEMS - 1, q, :], xin[:, q, :],
                                        ALU.add).then_inc(o_last, 1)

        @block.tensor
        def _(pe):
            def sj_rows(n, p):
                pe.wait_ge(s_copied, n + 1)
                for q in range(GPI):
                    last = nc.tensor.transpose(T[:, 0, q * P:(q + 1) * P],
                                               ssc[:, p, GPI + q:GPI + q + 1].to_broadcast([P, P]), ident[:, :])
                last.then_inc(sjb_ready, 1)

            def transpose_e(n):
                pe.wait_ge(exp_done, GPI * (n + 1))
                after(pe, h_act, 2 * KD * n)
                for q in range(GPI):
                    last = nc.tensor.transpose(T[:, 1, q * P:(q + 1) * P], e[:, q, :], ident[:, :])
                last.then_inc(et_ready, 1)

            def aggregate(n, g):
                pe.wait_ge(et_copied, n + 1)
                for q in range(GPI):
                    last = nc.tensor.matmul(T[:, q // PER, (q % PER) * D:(q % PER + 1) * D], eT[:, q, :],
                                            xs[:, g, q, :], start=True, stop=True, skip_group_check=True)
                    if q % PER == PER - 1:
                        last.then_inc(agg_ready, 1)

            def transpose_h(n):
                pe.wait_ge(n1_done, GPI * (n + 1))
                for k in range(KD):
                    for q in range(GPI):
                        last = nc.tensor.transpose(T[:, k, q * P:(q + 1) * P], r[:, q, k * P:(k + 1) * P], ident[:, :])
                    last.then_inc(ht_psum, 1)

            def w1(n, p, l, c, first):
                m = KH * n + c
                if first:
                    pe.wait_ge(w1_ready, KH * l + c + 1)
                if c == 0:
                    pe.wait_ge(h_act, 2 * KD * (n + 1))
                after(pe, gelu_done, 2 * (m - 1))
                cols = slice(c * P, (c + 1) * P)
                pairs = [(w, h, k) for w, h in ((W1hi, Hhi[p]), (W1lo, Hhi[p]), (W1hi, Hlo[p])) for k in range(KD)]
                for at_, (w, h, k) in enumerate(pairs):
                    if c == 0 and h is Hlo[p]:
                        pe.wait_ge(h_lo, KD * n + k + 1)
                    last = nc.tensor.matmul(U[:, c % 2, :], w[:, k, cols], h[:, k, :],
                                            start=(at_ == 0), stop=(at_ == len(pairs) - 1))
                last.then_inc(u_ready, 1)

            def w2(n, l, c, first):
                m = KH * n + c
                if first:
                    pe.wait_ge(w2_ready, KH * l + (c + 1 if c < KH - LAG - 1 else KH))
                if c == 0:
                    after(pe, ft_read, KD * n)
                pe.wait_ge(gelu_done, 2 * m + 2)
                wait_glo(pe, n, c)
                for k in range(KD):
                    cols = slice(k * P, (k + 1) * P)
                    pairs = ((W2hi, Ghi[c % 4]), (W2lo, Ghi[c % 4]), (W2hi, Glo[c % 4]))
                    for at_, (w, g) in enumerate(pairs):
                        last = nc.tensor.matmul(FT[:, k, :], w[:, c, cols], g[:, :], start=(c == 0 and at_ == 0),
                                                stop=(c == KH - 1 and at_ == len(pairs) - 1))
                    if c == KH - 1 and k == 0:
                        last.then_inc(ft0_ready, 1)
                last.then_inc(w2_done, 1)

            def transpose_back(n):
                pe.wait_ge(ft_read, KD * (n + 1))
                after(pe, f_free, GPI * n)
                for q in range(GPI):
                    for k in range(KD):
                        c0 = (q % PER) * D + k * P
                        last = nc.tensor.transpose(F[:, q // PER, c0:c0 + P], rT[:, k, q * P:(q + 1) * P], ident[:, :])
                    if q % PER == PER - 1:
                        last.then_inc(back_ready, 1)

            pe.wait_ge(s_id, 5)
            sj_rows(0, 0)
            transpose_e(0)
            aggregate(0, 0)
            transpose_h(0)
            pe.wait_ge(h_act, 2)
            sj_rows(1, 1)

            def body(l, i, p):
                n, nxt, far, prev = at(l, i, 0), at(l, i, 1), at(l, i, 2), at(l, i, -1)
                first = isinstance(i, int) and i == 0
                for c in range(KH):
                    w1(n, p, l, c, first)
                    if c == 0 and nxt is not None:
                        transpose_e(nxt)
                    if c >= LAG:
                        w2(n, l, c - LAG, first)
                    elif prev is not None:
                        w2(prev, layer(l, i, -1), KH - LAG + c, False)
                    if c == 1 and nxt is not None:
                        aggregate(nxt, group(l, i, 1))
                    if c == 2 and prev is not None:
                        transpose_back(prev)
                    if c == 4 and nxt is not None:
                        transpose_h(nxt)

            steps(pe, body)
            for c in range(KH - LAG, KH):
                w2(STEPS - 1, L - 1, c, False)
            transpose_back(STEPS - 1)


_INS = ['x', 'adj', 'L0_gnn_attn_w', 'L0_gnn_attn_b', 'L0_gnn_W1', 'L0_gnn_b1', 'L0_gnn_W2', 'L0_gnn_b2',
        'L0_gnn_g1', 'L0_gnn_beta1', 'L0_gnn_g2', 'L0_gnn_beta2']
_OUTS = [((64, 128, 256), 'float32')]


def kernel(**inputs):
    import numpy as _np
    import concourse.bacc as _bacc
    from concourse import mybir as _mybir
    from concourse.bass_utils import run_bass_kernel_spmd as _run

    nc = _bacc.Bacc("TRN2", target_bir_lowering=False, num_devices=1)
    arrays, args = {}, []
    for name in _INS:
        a = _np.ascontiguousarray(inputs[name])
        arrays[f"in_{name}_dram"] = a
        args.append(nc.dram_tensor(f"in_{name}_dram", a.shape, _mybir.dt.from_np(a.dtype), kind="ExternalInput").ap())
    for i, (shape, dtype) in enumerate(_OUTS):
        dt = _mybir.dt.from_np(_np.dtype(dtype))
        args.append(nc.dram_tensor(f"out_{i}_dram", shape, dt, kind="ExternalOutput").ap())
    gnn_kernel(nc, *args)
    r = _run(nc, [arrays], core_ids=[0])
    return r.results[0]["out_0_dram"]
```
